# Optimizing a Trainium2 kernel written in Bass

```python
import numpy as np
import jax
import jax.numpy as jnp

def _softmax(x, axis=-1):
    return jax.nn.softmax(x, axis=axis)
def _gelu(x):
    return jax.nn.gelu(x, approximate=True)
def _silu(x):
    return jax.nn.silu(x)
def _sigmoid(x):
    return jax.nn.sigmoid(x)
def _layernorm(x, axis=-1, eps=1e-5):
    m = jnp.mean(x, axis=axis, keepdims=True)
    v = jnp.var(x, axis=axis, keepdims=True)
    return (x - m) / jnp.sqrt(v + eps)
def _scatter_add(tgt, idx, src, axis=0):
    return tgt.at[idx].add(src)
def _segment_sum(src, seg, n):
    return jax.ops.segment_sum(src, seg, n)

kernel_name = 'mk_conv_seq_d1_conv_nchw256_7085b4'

def setup_inputs(seed: int = 0):
    np.random.seed(seed)
    _w = jnp.asarray
    def _rec_inputs():
        import jax
        import jax.numpy as jnp
        _gk = jax.random.key(seed)
        x = -0.0006128 + 1 * jax.random.normal(jax.random.fold_in(_gk, 1), (2, 256, 80, 80), jnp.float32)
        return x
    x = _rec_inputs()
    def _L0_conv_setup():
        import jax, jax.numpy as jnp
        import numpy as np
        CHANNEL = 256
        REDUCTION = 2
        CI = CHANNEL // REDUCTION
        B, H, W = (2, 80, 80)

        def _proj(x, w, b):
            return jnp.einsum('bchw,oc->bohw', x, w) + b[None, :, None, None]
        key = jax.random.key(seed)
        ks = jax.random.split(key, 9)
        s = 0.05
        return {'x': jax.random.normal(ks[0], (B, CHANNEL, H, W), jnp.float32), 'g_w': jax.random.normal(ks[1], (CI, CHANNEL), jnp.float32) * s, 'g_b': jax.random.normal(ks[2], (CI,), jnp.float32) * s, 'theta_w': jax.random.normal(ks[3], (CI, CHANNEL), jnp.float32) * s, 'theta_b': jax.random.normal(ks[4], (CI,), jnp.float32) * s, 'phi_w': jax.random.normal(ks[5], (CI, CHANNEL), jnp.float32) * s, 'phi_b': jax.random.normal(ks[6], (CI,), jnp.float32) * s, 'W_w': jax.random.normal(ks[7], (CHANNEL, CI), jnp.float32) * s, 'W_b': jax.random.normal(ks[8], (CHANNEL,), jnp.float32) * s}
    _L0_conv_all = _L0_conv_setup()
    _L0_conv_in = {k: v for k, v in _L0_conv_all.items() if k in ('g_w', 'g_b', 'theta_w', 'theta_b', 'phi_w', 'phi_b', 'W_w', 'W_b', )}
    del _L0_conv_all

    return {
        "x": x,
        "L0_conv_g_w": _L0_conv_in["g_w"],
        "L0_conv_g_b": _L0_conv_in["g_b"],
        "L0_conv_theta_w": _L0_conv_in["theta_w"],
        "L0_conv_theta_b": _L0_conv_in["theta_b"],
        "L0_conv_phi_w": _L0_conv_in["phi_w"],
        "L0_conv_phi_b": _L0_conv_in["phi_b"],
        "L0_conv_W_w": _L0_conv_in["W_w"],
        "L0_conv_W_b": _L0_conv_in["W_b"],
    }

def reference(x, L0_conv_g_w, L0_conv_g_b, L0_conv_theta_w, L0_conv_theta_b, L0_conv_phi_w, L0_conv_phi_b, L0_conv_W_w, L0_conv_W_b):
    import jax
    import jax.numpy as jnp
    def _L0_conv_ref(x, g_w, g_b, theta_w, theta_b, phi_w, phi_b, W_w, W_b):
        import jax, jax.numpy as jnp
        import numpy as np
        CHANNEL = 256
        REDUCTION = 2
        CI = CHANNEL // REDUCTION
        B, H, W = (2, 80, 80)

        def _proj(x, w, b):
            return jnp.einsum('bchw,oc->bohw', x, w) + b[None, :, None, None]
        b, c, h, w = x.shape
        n = h * w
        g_x = _proj(x, g_w, g_b).reshape(b, CI, n).transpose(0, 2, 1)
        theta_x = _proj(x, theta_w, theta_b).reshape(b, CI, n).transpose(0, 2, 1)
        phi_x = _proj(x, phi_w, phi_b).reshape(b, CI, n)
        f = jnp.einsum('bnc,bcm->bnm', theta_x, phi_x)
        f_div_C = jax.nn.softmax(f, axis=1)
        y = jnp.einsum('bnm,bmc->bnc', f_div_C, g_x)
        y = y.transpose(0, 2, 1).reshape(b, CI, h, w)
        W_y = _proj(y, W_w, W_b)
        return W_y + x

    def _gn(v, G=32, eps=1e-5):
        B_, C_, H_, W_ = v.shape
        g = v.reshape(B_, G, C_ // G, H_, W_)
        m = jnp.mean(g, axis=(2, 3, 4), keepdims=True)
        s = jnp.var(g, axis=(2, 3, 4), keepdims=True)
        return ((g - m) / jnp.sqrt(s + eps)).reshape(v.shape)

    def _ln_c(v, eps=1e-6):
        m = jnp.mean(v, axis=1, keepdims=True)
        s = jnp.var(v, axis=1, keepdims=True)
        return (v - m) / jnp.sqrt(s + eps)

    def _ln_t(v, eps=1e-5):
        m = jnp.mean(v, axis=-1, keepdims=True)
        s = jnp.var(v, axis=-1, keepdims=True)
        return (v - m) / jnp.sqrt(s + eps)

    def _to_tokens(v):
        B_, C_, H_, W_ = v.shape
        return v.reshape(B_, C_, H_ * W_).transpose(0, 2, 1)
    def _from_tokens(t, like):
        B_, C_, H_, W_ = like.shape
        return t.transpose(0, 2, 1).reshape(B_, C_, H_, W_)

    x = _L0_conv_ref(x, L0_conv_g_w, L0_conv_g_b, L0_conv_theta_w, L0_conv_theta_b, L0_conv_phi_w, L0_conv_phi_b, L0_conv_W_w, L0_conv_W_b)
    return x


_drawn_inputs = setup_inputs


def setup_inputs(seed=0):
    import zlib

    import numpy as np

    out = dict(_drawn_inputs(seed))
    spreads = {}
    factors = {}
    for name, (base, spread) in spreads.items():
        noise = np.random.default_rng([zlib.crc32(name.encode()), seed]).standard_normal(out[name].shape)
        drawn = base * np.exp(spread * noise) if base else spread * noise
        out[name] = jnp.asarray(drawn.astype(out[name].dtype))
    for name, factor in factors.items():
        out[name] = (out[name] * factor).astype(out[name].dtype)
    return out
```

```python
import concourse.bass as bass
from concourse import mybir
from contextlib import ExitStack


def build_non_local_block(nc, x, g_wT, g_b, theta_wT, theta_b, phi_wT, phi_b, out_wT, out_b, out):
    f32, f32r = mybir.dt.float32, mybir.dt.float32r
    ACT, ALU, AX = mybir.ActivationFunctionType, mybir.AluOpType, mybir.AxisListType

    B, C, H, W = x.shape
    N = H * W
    P = 128
    CI = theta_wT.shape[1]
    assert CI == P
    KC = C // P
    HB = C // P
    TILES = N // P
    BANK = 512
    HALF = 400
    STEP = 2 * HALF
    STEPS = N // STEP
    CHUNK = 2 * STEP
    CHUNKS = N // CHUNK
    PROJ_AT = 5
    RECIP_AT = 4
    STAGES = 3
    USES = STEPS + 1

    xf = x.rearrange("b (k p) h w -> b p k (h w)", p=P)
    outf = out.rearrange("b (k p) h w -> b p k (h w)", p=P)

    ctx = ExitStack()
    with ctx:
        def sb(name, shape, dt=f32):
            return ctx.enter_context(nc.sbuf_tensor(name, shape, dt))

        def sem(name):
            return ctx.enter_context(nc.semaphore(name))

        w_theta = sb("w_theta", [P, KC, CI])
        w_phi = sb("w_phi", [P, KC, CI])
        w_g = sb("w_g", [P, KC, CI])
        w_out = sb("w_out", [CI, C])
        bias_theta = sb("bias_theta", [P, 1])
        bias_phi = sb("bias_phi", [P, 1])
        bias_out = sb("bias_out", [P, HB])
        bias_g = sb("bias_g", [P, CI])

        theta_hi = sb("theta_hi", [CI, N], f32r)
        theta_lo = sb("theta_lo", [CI, N], f32r)
        y_sum = sb("y_sum", [CI, N])
        scores = [sb(f"scores{i}", [P, N]) for i in range(2)]
        probs_hi = sb("probs_hi", [P, N], f32r)
        probs_lo = sb("probs_lo", [P, N], f32r)
        stage = [sb(f"stage{i}", [P, KC, STEP]) for i in range(STAGES)]
        x_tile = [sb(f"x_tile{i}", [P, KC, P]) for i in range(2)]
        phi_full = sb("phi_full", [CI, P])
        phi_hi = [sb(f"phi_hi{i}", [CI, P], f32r) for i in range(2)]
        phi_lo = [sb(f"phi_lo{i}", [CI, P], f32r) for i in range(2)]
        g_full = [sb(f"g_full{i}", [P, CI]) for i in range(2)]
        g_scaled = sb("g_scaled", [P, CI])
        g_hi = [sb(f"g_hi{i}", [P, CI], f32r) for i in range(2)]
        g_lo = [sb(f"g_lo{i}", [P, CI], f32r) for i in range(2)]
        step_max = [sb(f"step_max{i}", [P, STEPS]) for i in range(2)]
        neg_max = [sb(f"neg_max{i}", [P, 1]) for i in range(2)]
        row_sum = [sb(f"row_sum{i}", [P, 1]) for i in range(2)]
        inv_sum = [sb(f"inv_sum{i}", [P, 1]) for i in range(2)]

        pair = [ctx.enter_context(nc.psum_tensor(f"pair{i}", [P, 2, BANK], f32)) for i in range(2)]
        y_pair = [ctx.enter_context(nc.psum_tensor(f"y_pair{i}", [P, 2, BANK], f32)) for i in range(2)]

        weights_in = sem("weights_in")
        x_tile_in = [sem(f"x_tile_in{i}") for i in range(2)]
        stage_in = [sem(f"stage_in{i}") for i in range(STAGES)]
        stage_out = [sem(f"stage_out{i}") for i in range(STAGES)]
        pair_filled = sem("pair_filled")
        pair_drained = sem("pair_drained")
        theta_hi_ready = sem("theta_hi_ready")
        phi_hi_ready = sem("phi_hi_ready")
        phi_ready = sem("phi_ready")
        max_ready = sem("max_ready")
        exp_done = sem("exp_done")
        inv_ready = sem("inv_ready")
        g_hi_ready = sem("g_hi_ready")
        g_ready = sem("g_ready")
        hi_ready = sem("hi_ready")
        lo_ready = sem("lo_ready")
        y_filled = sem("y_filled")
        y_added = sem("y_added")
        y_zeroed = sem("y_zeroed")

        LAST = B * TILES - 1
        assert STEPS % 2 == 0 and HB * STEPS % 2 == 0 and TILES % 2 == 0

        def extra(T):
            return sum(STEPS * (T >= b * TILES) + HB * STEPS * (T >= b * TILES + 2) for b in range(1, B))

        def period_base(T, e):
            return STEPS + 1 + USES * T + e

        def theta_base(b):
            return period_base(b * TILES, extra(b * TILES - 1)) if b else 0

        def output_base(b):
            T = (b + 1) * TILES
            return period_base(T + 2, extra(T + 1)) if b < B - 1 else period_base(T, extra(LAST)) - 1

        def projection(T, e):
            return period_base(T - 1, e) + PROJ_AT

        def use(T, j, e):
            late = j >= PROJ_AT and runs(T)[3]
            return period_base(T, e) + j + late

        def buffer(par, j, T):
            late = j >= PROJ_AT and runs(T)[3]
            return (STEPS + 1 + par * USES + j + late) % 2

        def runs(T):
            if not isinstance(T, int):
                return True, True, True, True
            return T <= LAST, 1 <= T <= LAST + 1, T >= 2, T < LAST

        def since(T, first):
            return not isinstance(T, int) or T >= first

        def schedule(period, theta, output, Fori):
            for b in range(B):
                theta(b)
                first = b * TILES
                period(first, 0, extra(first))
                period(first + 1, 1, extra(first + 1))
                if b:
                    output(b - 1)
                else:
                    period(first + 2, 0, 0)
                    period(first + 3, 1, 0)
                with Fori(first + 4 - 2 * b, first + TILES - 2 * (b == B - 1), 2) as T:
                    period(T, 0, extra(first + 2))
                    period(T + 1, 1, extra(first + 2))
            for T in range(LAST - 1, LAST + 3):
                period(T, T % 2, extra(LAST))
            output(B - 1)

        def banks(ap, j):
            return ap[:, j * STEP:(j + 1) * STEP].rearrange("p (h c) -> p h c", h=2)

        def chunk(ap, k):
            return ap[:, k * CHUNK:(k + 1) * CHUNK]

        def theta_stage(b, j):
            return STEPS * b + j

        def output_stage(b, j):
            return STEPS * (2 + b) + j

        assert B == 2

        WEIGHTS = 8
        block = ctx.enter_context(nc.Block())

        @block.sync
        def _(sp):
            def load_tile(b, t, par, e):
                T = b * TILES + t
                if since(T, 3):
                    sp.wait_ge(pair_drained, projection(T - 2, e) + 1)
                elif T == 2:
                    sp.wait_ge(pair_drained, STEPS + 1)
                sp.dma_start(x_tile[par][:, :, :], xf[b, :, :, bass.ds(t * P, P)]).then_inc(x_tile_in[par], 16)

            def load_stage(b, j, u):
                s = u % STAGES
                sp.dma_start(stage[s][:, :, :], xf[b, :, :, j * STEP:(j + 1) * STEP]).then_inc(stage_in[s], 16)

            def load_theta(b, j):
                u = theta_stage(b, j)
                if u >= STAGES:
                    ahead = theta_base(b) + j if j >= STAGES else theta_base(b - 1) + STEPS + j
                    sp.wait_ge(pair_filled, ahead - STAGES + 1)
                load_stage(b, j, u)

            def stores_before(u):
                first = output_stage(0, 0)
                return 16 * sum(v % STAGES == u % STAGES for v in range(first, u))

            def load_residual(b, j):
                u = output_stage(b, j)
                if stores_before(u):
                    sp.wait_ge(stage_out[u % STAGES], stores_before(u))
                else:
                    sp.wait_ge(pair_filled, theta_base(B - 1) + STEPS + j - STAGES + 1)
                load_stage(b, j, u)

            def output(b):
                for j in range(STEPS):
                    s = output_stage(b, j) % STAGES
                    sp.wait_ge(pair_drained, output_base(b) + HB * (j + 1))
                    sp.dma_start(outf[b, :, :, j * STEP:(j + 1) * STEP], stage[s][:, :, :]
                                 ).then_inc(stage_out[s], 16)
                    if j >= 1 and j - 1 + STAGES < STEPS:
                        load_residual(b, j - 1 + STAGES)

            load_theta(0, 0)
            load_tile(0, 0, 0, 0)
            load_tile(0, 1, 1, 0)
            for j in range(1, STEPS):
                load_theta(0, j)
            for j in range(STAGES):
                load_theta(1, j)
            load_tile(0, 2, 0, 0)
            load_tile(0, 3, 1, 0)
            with sp.Fori(4, TILES - 1, 2) as t:
                load_tile(0, t, 0, 0)
                load_tile(0, t + 1, 1, 0)
            for t in range(3):
                load_tile(1, t, t % 2, extra(TILES + t - 3))
            for j in range(STAGES, STEPS):
                load_theta(1, j)
            for j in range(STAGES):
                load_residual(0, j)
            for t in (3, 4):
                load_tile(1, t, t % 2, extra(TILES + t - 3))
            output(0)
            load_tile(1, 5, 1, extra(TILES + 2))
            with sp.Fori(6, TILES - 1, 2) as t:
                load_tile(1, t, 0, extra(TILES + 2))
                load_tile(1, t + 1, 1, extra(TILES + 2))
            for j in range(STAGES):
                load_residual(1, j)
            output(1)
            for s in range(STAGES):
                u = output_stage(B - 1, STEPS) + (s - output_stage(B - 1, STEPS)) % STAGES
                sp.wait_ge(stage_out[s], stores_before(u))

        @block.tensor
        def _(pe):
            def await_pair(n):
                if since(n, 2):
                    pe.wait_ge(pair_drained, n - 1)

            def product(into, parts, at):
                for i, (stationary, moving) in enumerate(parts):
                    for h in range(2):
                        last = nc.tensor.matmul(into[:, h, 0:HALF], stationary[:, :],
                                                moving[:, at + h * HALF:at + (h + 1) * HALF],
                                                start=i == 0, stop=i == len(parts) - 1)
                return last

            def project(T, par, n, buf):
                await_pair(n)
                pe.wait_ge(x_tile_in[par], (T - par) * 8 + 16)
                for k in range(KC):
                    nc.tensor.matmul(pair[buf][:, 0, 0:P], w_phi[:, k, :], x_tile[par][:, k, :],
                                     start=k == 0, stop=k == KC - 1)
                for k in range(KC):
                    last = nc.tensor.matmul(pair[buf][:, 1, 0:CI], x_tile[par][:, k, :], w_g[:, k, :],
                                            start=k == 0, stop=k == KC - 1)
                last.then_inc(pair_filled, 1)

            def period(T, par, e):
                own, _, products, proj = runs(T)
                for j in range(STEPS):
                    if j == PROJ_AT and proj:
                        project(T + 1, 1 - par, period_base(T, e) + PROJ_AT,
                                (STEPS + 1 + par * USES + PROJ_AT) % 2)
                    if own:
                        await_pair(use(T, j, e))
                        if j == 0:
                            pe.wait_ge(phi_ready, T + 1)
                        if isinstance(T, int) and T % TILES == 0:
                            pe.wait_ge(pair_drained, theta_base(T // TILES) + j + 1)
                        parts = ((phi_lo[par], theta_hi), (phi_hi[par], theta_lo), (phi_hi[par], theta_hi))
                        product(pair[buffer(par, j, T)], parts, j * STEP).then_inc(pair_filled, 1)
                    if products:
                        if j == 0:
                            pe.wait_ge(g_ready, T - 1)
                        if j % 2 == 0:
                            pe.wait_ge(lo_ready, (T - 2) * CHUNKS + j // 2 + 1)
                        if since(T, 3) or j >= 2:
                            pe.wait_ge(y_added, (T - 2) * STEPS + j - 1)
                        parts = ((g_lo[par], probs_hi), (g_hi[par], probs_lo), (g_hi[par], probs_hi))
                        product(y_pair[j % 2], parts, j * STEP).then_inc(y_filled, 1)

            def theta(b):
                if b == 0:
                    pe.wait_ge(weights_in, 16 * WEIGHTS)
                for j in range(STEPS):
                    n, u = theta_base(b) + j, theta_stage(b, j)
                    await_pair(n)
                    pe.wait_ge(stage_in[u % STAGES], 16 * (u // STAGES + 1))
                    for k in range(KC):
                        for h in range(2):
                            last = nc.tensor.matmul(pair[n % 2][:, h, 0:HALF], w_theta[:, k, :],
                                                    stage[u % STAGES][:, k, h * HALF:(h + 1) * HALF],
                                                    start=k == 0, stop=k == KC - 1)
                    last.then_inc(pair_filled, 1)
                if b == 0:
                    project(0, 0, STEPS, STEPS % 2)

            def output(b):
                pe.wait_ge(y_added, (b + 1) * TILES * STEPS)
                for j in range(STEPS):
                    for o in range(HB):
                        n = output_base(b) + HB * j + o
                        await_pair(n)
                        for h in range(2):
                            at = j * STEP + h * HALF
                            last = nc.tensor.matmul(pair[n % 2][:, h, 0:HALF], w_out[:, o * P:(o + 1) * P],
                                                    y_sum[:, at:at + HALF], start=True, stop=True)
                        last.then_inc(pair_filled, 1)

            schedule(period, theta, output, pe.Fori)

        @block.scalar
        def _(act):
            for dst, src in ((w_theta, theta_wT), (w_phi, phi_wT), (w_g, g_wT)):
                act.dma_start(dst[:, :, :], src.rearrange("(k p) c -> p k c", p=P)).then_inc(weights_in, 16)
            act.dma_start(w_out[:, :], out_wT).then_inc(weights_in, 16)
            act.dma_start(bias_theta[:, :], theta_b.rearrange("(p a) -> p a", a=1)).then_inc(weights_in, 16)
            act.dma_start(bias_phi[:, :], phi_b.rearrange("(p a) -> p a", a=1)).then_inc(weights_in, 16)
            act.dma_start(bias_out[:, :], out_b).then_inc(weights_in, 16)
            act.dma_start(bias_g[:, :], g_b.partition_broadcast(P)).then_inc(weights_in, 16)

            def round_hi(U, q, k):
                act.wait_ge(exp_done, U + 1)
                if since(U, 1):
                    act.wait_ge(y_filled, (U - 1) * STEPS + 2 * k + 2)
                nc.scalar.activation(chunk(probs_hi, k), chunk(scores[q], k), ACT.Copy).then_inc(hi_ready, 1)

            def round_phi(T, par, n):
                act.wait_ge(pair_drained, n + 1)
                nc.scalar.activation(phi_hi[par][:, :], phi_full[:, :], ACT.Copy).then_inc(phi_hi_ready, 1)

            def scale_g(U, q):
                act.wait_ge(inv_ready, U + 1)
                if since(U, 1):
                    act.wait_ge(g_ready, U)
                nc.scalar.activation(g_scaled[:, :], g_full[q][:, :], ACT.Copy, scale=inv_sum[q][:, :])
                if since(U, 2):
                    act.wait_ge(y_filled, (U - 1) * STEPS)
                nc.scalar.activation(g_hi[q][:, :], g_full[q][:, :], ACT.Copy,
                                     scale=inv_sum[q][:, :]).then_inc(g_hi_ready, 1)

            def period(T, par, e):
                _, softmax, _, proj = runs(T)
                U, q = T - 1, 1 - par
                if softmax:
                    act.wait_ge(max_ready, U + 1)
                    nc.scalar.activation(scores[q][:, :], scores[q][:, :], ACT.Exp, bias=neg_max[q][:, :],
                                         accum_out=row_sum[q][:, :]).then_inc(exp_done, 1)
                    round_hi(U, q, 0)
                    scale_g(U, q)
                    round_hi(U, q, 1)
                if proj:
                    round_phi(T + 1, 1 - par, projection(T + 1, e))
                if softmax:
                    round_hi(U, q, 2)
                    round_hi(U, q, 3)

            def theta(b):
                if b == 0:
                    act.wait_ge(weights_in, 16 * WEIGHTS)
                for j in range(STEPS):
                    n = theta_base(b) + j
                    act.wait_ge(pair_filled, n + 1)
                    nc.scalar.activation(banks(theta_hi, j), pair[n % 2][:, :, 0:HALF], ACT.Identity,
                                         bias=bias_theta[:, :]).then_inc(theta_hi_ready, 1)
                if b == 0:
                    round_phi(0, 0, STEPS)

            def output(b):
                pass

            schedule(period, theta, output, act.Fori)

        @block.gpsimd
        def _(pool):
            def lo_part(U, q, k):
                pool.wait_ge(hi_ready, U * CHUNKS + k + 1)
                nc.gpsimd.tensor_tensor(chunk(probs_lo, k), chunk(scores[q], k),
                                        chunk(probs_hi, k).bitcast(f32), ALU.subtract).then_inc(lo_ready, 1)

            def phi_part(T, par):
                pool.wait_ge(phi_hi_ready, T + 1)
                nc.gpsimd.tensor_tensor(phi_lo[par][:, :], phi_full[:, :], phi_hi[par][:, :].bitcast(f32),
                                        ALU.subtract).then_inc(phi_ready, 1)

            def zero_y():
                for k in range(CHUNKS):
                    nc.gpsimd.memset(chunk(y_sum, k), 0.0).then_inc(y_zeroed, 1)

            def period(T, par, e):
                _, softmax, _, proj = runs(T)
                U, q = T - 1, 1 - par
                if softmax:
                    lo_part(U, q, 0)
                    pool.wait_ge(g_hi_ready, U + 1)
                    nc.gpsimd.tensor_tensor(g_lo[q][:, :], g_scaled[:, :], g_hi[q][:, :].bitcast(f32),
                                            ALU.subtract).then_inc(g_ready, 1)
                if proj:
                    phi_part(T + 1, 1 - par)
                if softmax:
                    for k in range(1, CHUNKS):
                        lo_part(U, q, k)

            def theta(b):
                if b == 0:
                    zero_y()
                    phi_part(0, 0)

            def output(b):
                if b < B - 1:
                    for k in range(CHUNKS):
                        pool.wait_ge(pair_filled, output_base(b) + HB * 2 * (k + 1))
                        nc.gpsimd.memset(chunk(y_sum, k), 0.0).then_inc(y_zeroed, 1)

            schedule(period, theta, output, pool.Fori)

        @block.vector
        def _(dve):
            def take_projection(T, par, n, buf):
                dve.wait_ge(pair_filled, n + 1)
                if since(T, 2):
                    dve.wait_ge(g_hi_ready, T - 1)
                nc.vector.tensor_tensor(g_full[par][:, :], pair[buf][:, 1, 0:CI], bias_g[:, :], ALU.add)
                if since(T, 1):
                    dve.wait_ge(phi_ready, T)
                nc.vector.tensor_scalar(phi_full[:, :], pair[buf][:, 0, 0:P], bias_phi[:, :], None,
                                        ALU.add).then_inc(pair_drained, 1)

            def period(T, par, e):
                own, softmax, products, proj = runs(T)
                for j in range(STEPS):
                    if j == RECIP_AT and softmax:
                        dve.wait_ge(exp_done, T)
                        nc.vector.reciprocal(inv_sum[1 - par][:, :], row_sum[1 - par][:, :]).then_inc(inv_ready, 1)
                    if j == PROJ_AT and proj:
                        take_projection(T + 1, 1 - par, period_base(T, e) + PROJ_AT,
                                        (STEPS + 1 + par * USES + PROJ_AT) % 2)
                    if own:
                        dve.wait_ge(pair_filled, use(T, j, e) + 1)
                        if since(T, 2) and j % 2 == 0:
                            dve.wait_ge(lo_ready, (T - 2) * CHUNKS + j // 2 + 1)
                        nc.vector.tensor_scalar(banks(scores[par], j), pair[buffer(par, j, T)][:, :, 0:HALF],
                                                0.0, None, ALU.add, ALU.max,
                                                accum_out=step_max[par][:, j:j + 1]).then_inc(pair_drained, 1)
                    if products:
                        dve.wait_ge(y_filled, (T - 2) * STEPS + j + 1)
                        nc.vector.tensor_tensor(banks(y_sum, j), y_pair[j % 2][:, :, 0:HALF], banks(y_sum, j),
                                                ALU.add).then_inc(y_added, 1)
                if own:
                    dve.wait_ge(pair_drained, use(T, STEPS - 1, e) + 1)
                    nc.vector.tensor_reduce(neg_max[par][:, :], step_max[par][:, :], AX.X, ALU.max,
                                            negate=True).then_inc(max_ready, 1)

            def theta(b):
                if b == 0:
                    dve.wait_ge(weights_in, 16 * WEIGHTS)
                for j in range(STEPS):
                    n = theta_base(b) + j
                    dve.wait_ge(theta_hi_ready, b * STEPS + j + 1)
                    nc.vector.scalar_tensor_tensor(out=banks(theta_lo, j), in0=pair[n % 2][:, :, 0:HALF],
                                                   scalar=bias_theta[:, :], in1=banks(theta_hi, j).bitcast(f32),
                                                   op0=ALU.add, op1=ALU.subtract).then_inc(pair_drained, 1)
                if b == 0:
                    take_projection(0, 0, STEPS, STEPS % 2)
                    dve.wait_ge(y_zeroed, CHUNKS)

            def output(b):
                for j in range(STEPS):
                    u = output_stage(b, j)
                    dve.wait_ge(stage_in[u % STAGES], 16 * (u // STAGES + 1))
                    for o in range(HB):
                        n = output_base(b) + HB * j + o
                        dve.wait_ge(pair_filled, n + 1)
                        columns = stage[u % STAGES][:, o, :].rearrange("p (h c) -> p h c", h=2)
                        nc.vector.scalar_tensor_tensor(out=columns, in0=pair[n % 2][:, :, 0:HALF],
                                                       scalar=bias_out[:, o:o + 1], in1=columns,
                                                       op0=ALU.add, op1=ALU.add).then_inc(pair_drained, 1)
                if b < B - 1:
                    dve.wait_ge(y_zeroed, CHUNKS * (b + 2))

            schedule(period, theta, output, dve.Fori)


_OUT = ((2, 256, 80, 80), 'float32')


def kernel(x, L0_conv_g_w, L0_conv_g_b, L0_conv_theta_w, L0_conv_theta_b, L0_conv_phi_w, L0_conv_phi_b,
           L0_conv_W_w, L0_conv_W_b):
    import numpy as _np
    import concourse.bacc as _bacc
    from concourse import mybir as _mybir
    from concourse.bass_utils import run_bass_kernel_spmd as _run

    nc = _bacc.Bacc("TRN2", target_bir_lowering=False, num_devices=1)
    given = {
        "x": x, "g_wT": L0_conv_g_w.T, "g_b": L0_conv_g_b, "theta_wT": L0_conv_theta_w.T,
        "theta_b": L0_conv_theta_b, "phi_wT": L0_conv_phi_w.T, "phi_b": L0_conv_phi_b,
        "out_wT": L0_conv_W_w.T, "out_b": L0_conv_W_b.reshape(-1, 128).T,
    }
    arrays, args = {}, []
    for name, value in given.items():
        a = _np.ascontiguousarray(value)
        arrays[f"in_{name}_dram"] = a
        args.append(nc.dram_tensor(f"in_{name}_dram", a.shape, _mybir.dt.from_np(a.dtype), kind="ExternalInput").ap())
    shape, dtype = _OUT
    args.append(nc.dram_tensor("out_0_dram", shape, _mybir.dt.from_np(_np.dtype(dtype)), kind="ExternalOutput").ap())
    build_non_local_block(nc, *args)
    r = _run(nc, [arrays], core_ids=[0])
    return r.results[0]["out_0_dram"]
```

```python
import concourse.bass as bass
from concourse import mybir
from contextlib import ExitStack


def build_non_local_block(nc, x, g_wT, g_b, theta_wT, theta_b, phi_wT, phi_b, out_wT, out_b, out):
    f32, f32r = mybir.dt.float32, mybir.dt.float32r
    ACT, ALU, AX = mybir.ActivationFunctionType, mybir.AluOpType, mybir.AxisListType

    B, C, H, W = x.shape
    N = H * W
    P = 128
    CI = theta_wT.shape[1]
    assert CI == P
    KC = C // P
    HB = C // P
    TILES = N // P
    BANK = 512
    HALF = 400
    STEP = 2 * HALF
    STEPS = N // STEP
    CHUNK = 2 * STEP
    CHUNKS = N // CHUNK
    PROJ_AT = 5
    RECIP_AT = 4
    STAGES = 6
    BLOCKS = N // HALF
    USES = STEPS + 1

    xf = x.rearrange("b (k p) h w -> b p k (h w)", p=P)
    outf = out.rearrange("b (k p) h w -> b p k (h w)", p=P)

    ctx = ExitStack()
    with ctx:
        def sb(name, shape, dt=f32):
            return ctx.enter_context(nc.sbuf_tensor(name, shape, dt))

        def sem(name):
            return ctx.enter_context(nc.semaphore(name))

        w_theta = sb("w_theta", [P, KC, CI])
        w_phi = sb("w_phi", [P, KC, CI])
        w_g = sb("w_g", [P, KC, CI])
        w_out = sb("w_out", [CI, C])
        bias_theta = sb("bias_theta", [P, 1])
        bias_phi = sb("bias_phi", [P, 1])
        bias_out = sb("bias_out", [P, HB])
        bias_g = sb("bias_g", [P, CI])

        theta_hi = sb("theta_hi", [CI, N], f32r)
        theta_lo = sb("theta_lo", [CI, N], f32r)
        y_sum = sb("y_sum", [CI, N])
        scores = [sb(f"scores{i}", [P, N]) for i in range(2)]
        probs_hi = sb("probs_hi", [P, N], f32r)
        probs_lo = sb("probs_lo", [P, N], f32r)
        stage = [sb(f"stage{i}", [P, KC, HALF]) for i in range(STAGES)]
        x_tile = [sb(f"x_tile{i}", [P, KC, P]) for i in range(2)]
        phi_full = sb("phi_full", [CI, P])
        phi_hi = [sb(f"phi_hi{i}", [CI, P], f32r) for i in range(2)]
        phi_lo = [sb(f"phi_lo{i}", [CI, P], f32r) for i in range(2)]
        g_full = [sb(f"g_full{i}", [P, CI]) for i in range(2)]
        g_scaled = sb("g_scaled", [P, CI])
        g_hi = [sb(f"g_hi{i}", [P, CI], f32r) for i in range(2)]
        g_lo = [sb(f"g_lo{i}", [P, CI], f32r) for i in range(2)]
        step_max = [sb(f"step_max{i}", [P, STEPS]) for i in range(2)]
        neg_max = [sb(f"neg_max{i}", [P, 1]) for i in range(2)]
        row_sum = [sb(f"row_sum{i}", [P, 1]) for i in range(2)]
        inv_sum = [sb(f"inv_sum{i}", [P, 1]) for i in range(2)]

        pair = [ctx.enter_context(nc.psum_tensor(f"pair{i}", [P, 2, BANK], f32)) for i in range(2)]
        y_pair = [ctx.enter_context(nc.psum_tensor(f"y_pair{i}", [P, 2, BANK], f32)) for i in range(2)]

        theta_weights_in = sem("theta_weights_in")
        weights_in = sem("weights_in")
        x_tile_in = [sem(f"x_tile_in{i}") for i in range(2)]
        stage_in = [sem(f"stage_in{i}") for i in range(STAGES)]
        stage_out = [sem(f"stage_out{i}") for i in range(STAGES)]
        pair_filled = sem("pair_filled")
        pair_drained = sem("pair_drained")
        theta_hi_ready = sem("theta_hi_ready")
        phi_hi_ready = sem("phi_hi_ready")
        phi_ready = sem("phi_ready")
        max_ready = sem("max_ready")
        exp_done = sem("exp_done")
        inv_ready = sem("inv_ready")
        g_hi_ready = sem("g_hi_ready")
        g_ready = sem("g_ready")
        hi_ready = sem("hi_ready")
        lo_ready = sem("lo_ready")
        y_filled = sem("y_filled")
        y_added = sem("y_added")
        last_lo_ready = sem("last_lo_ready")

        LAST = B * TILES - 1
        assert STEPS % 2 == 0 and HB * STEPS % 2 == 0 and TILES % 2 == 0

        WEIGHTS = 6

        def output_in(T):
            known = isinstance(T, int) and T > TILES and T <= LAST
            return T // TILES - 1 if known and T % TILES == 2 else None

        def runs(T):
            if not isinstance(T, int):
                return True, True, True, True
            return T <= LAST, 1 <= T <= LAST + 1, T >= 2, T < LAST

        def is_last(T):
            return isinstance(T, int) and T == LAST + 2

        def since(T, first):
            return not isinstance(T, int) or T >= first

        def extra(T):
            return sum(STEPS * (T >= b * TILES) + HB * STEPS * (T > b * TILES + 2) for b in range(1, B))

        def period_base(T, e):
            return STEPS + 1 + USES * T + e

        def theta_base(b):
            return period_base(b * TILES, extra(b * TILES - 1)) if b else 0

        def outputs_ahead(T, j):
            return 0 if output_in(T) is None else HB * j

        def projection(T, e):
            return period_base(T - 1, e) + PROJ_AT + outputs_ahead(T - 1, PROJ_AT)

        def use(T, j, e):
            late = j >= PROJ_AT and runs(T)[3]
            return period_base(T, e) + j + late + outputs_ahead(T, j + 1)

        def output_use(b, j, o):
            T = (b + 1) * TILES + 2
            if b < B - 1:
                return use(T, j, extra(T)) - HB + o
            return period_base(LAST + 1, extra(LAST)) - 1 + HB * j + o

        def buffer(par, idx):
            return (STEPS + 1 + par * USES + idx) % 2

        def step_buffer(T, par, j):
            return buffer(par, j + (j >= PROJ_AT and runs(T)[3]))

        def schedule(period, theta, Fori):
            for b in range(B):
                theta(b)
                first = b * TILES
                for T in range(first, first + 4):
                    period(T, T % 2, extra(T))
                with Fori(first + 4, first + TILES - 2 * (b == B - 1), 2) as T:
                    period(T, 0, extra(first + 4))
                    period(T + 1, 1, extra(first + 4))
            for T in range(LAST - 1, LAST + 3):
                period(T, T % 2, extra(LAST))

        def banks(ap, j):
            return ap[:, j * STEP:(j + 1) * STEP].rearrange("p (h c) -> p h c", h=2)

        def chunk(ap, k):
            return ap[:, k * CHUNK:(k + 1) * CHUNK]

        def theta_stage(b, i):
            return BLOCKS * b + i

        def output_stage(b, i):
            return BLOCKS * (2 + b) + i

        assert B == 2

        block = ctx.enter_context(nc.Block())

        @block.sync
        def _(sp):
            def load_tile(b, t, par):
                T = b * TILES + t
                if since(T, 2):
                    sp.wait_ge(phi_ready, T - 1)
                sp.dma_start(x_tile[par][:, :, :], xf[b, :, :, bass.ds(t * P, P)]).then_inc(x_tile_in[par], 16)

            def load_stage(b, i, u):
                s = u % STAGES
                sp.dma_start(stage[s][:, :, :], xf[b, :, :, i * HALF:(i + 1) * HALF]).then_inc(stage_in[s], 16)

            def load_theta(b, i):
                u = theta_stage(b, i)
                if u >= STAGES:
                    n = u - STAGES
                    sp.wait_ge(pair_filled, theta_base(n // BLOCKS) + n % BLOCKS // 2 + 1)
                load_stage(b, i, u)

            def stores_before(u):
                return 16 * sum(v % STAGES == u % STAGES for v in range(output_stage(0, 0), u))

            def load_residual(b, i):
                u = output_stage(b, i)
                if stores_before(u):
                    sp.wait_ge(stage_out[u % STAGES], stores_before(u))
                else:
                    sp.wait_ge(pair_filled, theta_base(B - 1) + (BLOCKS + i - STAGES) // 2 + 1)
                load_stage(b, i, u)

            def output(b):
                for i in range(BLOCKS):
                    s = output_stage(b, i) % STAGES
                    sp.wait_ge(pair_drained, output_use(b, i // 2, HB - 1) + 1)
                    sp.dma_start(outf[b, :, :, i * HALF:(i + 1) * HALF], stage[s][:, :, :]
                                 ).then_inc(stage_out[s], 16)
                    if i >= 1 and i - 1 + STAGES < BLOCKS:
                        load_residual(b, i - 1 + STAGES)

            load_theta(0, 0)
            load_tile(0, 0, 0)
            load_tile(0, 1, 1)
            for i in range(1, BLOCKS):
                load_theta(0, i)
            for i in range(STAGES):
                load_theta(1, i)
            load_tile(0, 2, 0)
            load_tile(0, 3, 1)
            with sp.Fori(4, TILES - 1, 2) as t:
                load_tile(0, t, 0)
                load_tile(0, t + 1, 1)
            for t in range(3):
                load_tile(1, t, t % 2)
            for i in range(STAGES, BLOCKS):
                load_theta(1, i)
            for i in range(STAGES):
                load_residual(0, i)
            for t in (3, 4):
                load_tile(1, t, t % 2)
            output(0)
            load_tile(1, 5, 1)
            with sp.Fori(6, TILES - 1, 2) as t:
                load_tile(1, t, 0)
                load_tile(1, t + 1, 1)
            for i in range(STAGES):
                load_residual(1, i)
            output(1)
            for s in range(STAGES):
                u = output_stage(B - 1, BLOCKS) + (s - output_stage(B - 1, BLOCKS)) % STAGES
                sp.wait_ge(stage_out[s], stores_before(u))

        @block.tensor
        def _(pe):
            def await_pair(n):
                if since(n, 2):
                    pe.wait_ge(pair_drained, n - 1)

            def product(into, parts, at):
                for i, (stationary, moving) in enumerate(parts):
                    for h in range(2):
                        last = nc.tensor.matmul(into[:, h, 0:HALF], stationary[:, :],
                                                moving[:, at + h * HALF:at + (h + 1) * HALF],
                                                start=i == 0, stop=i == len(parts) - 1)
                return last

            def project(T, par, n, buf):
                await_pair(n)
                pe.wait_ge(x_tile_in[par], (T - par) * 8 + 16)
                for k in range(KC):
                    nc.tensor.matmul(pair[buf][:, 0, 0:P], w_phi[:, k, :], x_tile[par][:, k, :],
                                     start=k == 0, stop=k == KC - 1)
                for k in range(KC):
                    last = nc.tensor.matmul(pair[buf][:, 1, 0:CI], x_tile[par][:, k, :], w_g[:, k, :],
                                            start=k == 0, stop=k == KC - 1)
                last.then_inc(pair_filled, 1)

            def output_step(b, j):
                for o in range(HB):
                    n = output_use(b, j, o)
                    await_pair(n)
                    for h in range(2):
                        at = j * STEP + h * HALF
                        last = nc.tensor.matmul(pair[n % 2][:, h, 0:HALF], w_out[:, o * P:(o + 1) * P],
                                                y_sum[:, at:at + HALF], start=True, stop=True)
                    last.then_inc(pair_filled, 1)

            def last_output_step(j):
                pe.wait_ge(y_added, LAST * STEPS + j + 1)
                output_step(B - 1, j)

            def period(T, par, e):
                own, _, products, proj = runs(T)
                for j in range(STEPS):
                    if j == PROJ_AT and proj:
                        project(T + 1, 1 - par, projection(T + 1, e), buffer(par, PROJ_AT))
                    if output_in(T) is not None:
                        pe.wait_ge(y_added, (T - 2) * STEPS)
                        output_step(output_in(T), j)
                    if own:
                        await_pair(use(T, j, e))
                        if j == 0:
                            pe.wait_ge(phi_ready, T + 1)
                        if isinstance(T, int) and T % TILES == 0:
                            pe.wait_ge(pair_drained, theta_base(T // TILES) + j + 1)
                        parts = ((phi_lo[par], theta_hi), (phi_hi[par], theta_lo), (phi_hi[par], theta_hi))
                        product(pair[step_buffer(T, par, j)], parts, j * STEP).then_inc(pair_filled, 1)
                    if products:
                        if j == 0:
                            pe.wait_ge(g_ready, T - 1)
                        if j % 2 == 0 and is_last(T):
                            pe.wait_ge(last_lo_ready, j // 2 + 1)
                        elif j % 2 == 0:
                            pe.wait_ge(lo_ready, (T - 2) * CHUNKS + j // 2 + 1)
                        if since(T, 3) or j >= 2:
                            pe.wait_ge(y_added, (T - 2) * STEPS + j - 1)
                        parts = ((g_lo[par], probs_hi), (g_hi[par], probs_lo), (g_hi[par], probs_hi))
                        product(y_pair[j % 2], parts, j * STEP).then_inc(y_filled, 1)
                    if is_last(T) and j:
                        last_output_step(j - 1)
                if is_last(T):
                    last_output_step(STEPS - 1)

            def theta(b):
                if b == 0:
                    pe.wait_ge(theta_weights_in, 32)
                for j in range(STEPS):
                    n = theta_base(b) + j
                    await_pair(n)
                    for h in range(2):
                        u = theta_stage(b, 2 * j + h)
                        pe.wait_ge(stage_in[u % STAGES], 16 * (u // STAGES + 1))
                        for k in range(KC):
                            last = nc.tensor.matmul(pair[n % 2][:, h, 0:HALF], w_theta[:, k, :],
                                                    stage[u % STAGES][:, k, :],
                                                    start=k == 0, stop=k == KC - 1)
                    last.then_inc(pair_filled, 1)
                if b == 0:
                    pe.wait_ge(weights_in, 16 * WEIGHTS)
                    project(0, 0, STEPS, STEPS % 2)

            schedule(period, theta, pe.Fori)

        @block.scalar
        def _(act):
            def load_weight(dst, src):
                return act.dma_start(dst[:, :, :], src.rearrange("(k p) c -> p k c", p=P))

            load_weight(w_theta, theta_wT).then_inc(theta_weights_in, 16)
            act.dma_start(bias_theta[:, :], theta_b.rearrange("(p a) -> p a", a=1)).then_inc(theta_weights_in, 16)
            load_weight(w_phi, phi_wT).then_inc(weights_in, 16)
            load_weight(w_g, g_wT).then_inc(weights_in, 16)
            act.dma_start(w_out[:, :], out_wT).then_inc(weights_in, 16)
            act.dma_start(bias_phi[:, :], phi_b.rearrange("(p a) -> p a", a=1)).then_inc(weights_in, 16)
            act.dma_start(bias_out[:, :], out_b).then_inc(weights_in, 16)
            act.dma_start(bias_g[:, :], g_b.partition_broadcast(P)).then_inc(weights_in, 16)

            def round_hi(U, q, k):
                act.wait_ge(exp_done, U + 1)
                if since(U, 1):
                    act.wait_ge(y_filled, (U - 1) * STEPS + 2 * k + 2)
                nc.scalar.activation(chunk(probs_hi, k), chunk(scores[q], k), ACT.Copy).then_inc(hi_ready, 1)

            def round_phi(T, par, n):
                act.wait_ge(pair_drained, n + 1)
                nc.scalar.activation(phi_hi[par][:, :], phi_full[:, :], ACT.Copy).then_inc(phi_hi_ready, 1)

            def scale_g(U, q):
                act.wait_ge(inv_ready, U + 1)
                if since(U, 1):
                    act.wait_ge(g_ready, U)
                nc.scalar.activation(g_scaled[:, :], g_full[q][:, :], ACT.Copy, scale=inv_sum[q][:, :])
                if since(U, 2):
                    act.wait_ge(y_filled, (U - 1) * STEPS)
                nc.scalar.activation(g_hi[q][:, :], g_full[q][:, :], ACT.Copy,
                                     scale=inv_sum[q][:, :]).then_inc(g_hi_ready, 1)

            def period(T, par, e):
                _, softmax, _, proj = runs(T)
                U, q = T - 1, 1 - par
                if softmax:
                    act.wait_ge(max_ready, U + 1)
                    nc.scalar.activation(scores[q][:, :], scores[q][:, :], ACT.Exp, bias=neg_max[q][:, :],
                                         accum_out=row_sum[q][:, :]).then_inc(exp_done, 1)
                    round_hi(U, q, 0)
                    scale_g(U, q)
                    round_hi(U, q, 1)
                if proj:
                    round_phi(T + 1, 1 - par, projection(T + 1, e))
                if softmax:
                    round_hi(U, q, 2)
                    round_hi(U, q, 3)

            def theta(b):
                if b == 0:
                    act.wait_ge(theta_weights_in, 32)
                for j in range(STEPS):
                    n = theta_base(b) + j
                    act.wait_ge(pair_filled, n + 1)
                    nc.scalar.activation(banks(theta_hi, j), pair[n % 2][:, :, 0:HALF], ACT.Identity,
                                         bias=bias_theta[:, :]).then_inc(theta_hi_ready, 1)
                if b == 0:
                    round_phi(0, 0, STEPS)

            schedule(period, theta, act.Fori)

        @block.gpsimd
        def _(pool):
            def lo_part(U, q, k):
                pool.wait_ge(hi_ready, U * CHUNKS + k + 1)
                nc.gpsimd.tensor_tensor(chunk(probs_lo, k), chunk(scores[q], k),
                                        chunk(probs_hi, k).bitcast(f32), ALU.subtract).then_inc(lo_ready, 1)

            def phi_part(T, par):
                pool.wait_ge(phi_hi_ready, T + 1)
                nc.gpsimd.tensor_tensor(phi_lo[par][:, :], phi_full[:, :], phi_hi[par][:, :].bitcast(f32),
                                        ALU.subtract).then_inc(phi_ready, 1)

            def period(T, par, e):
                _, softmax, _, proj = runs(T)
                U, q = T - 1, 1 - par
                lo_parts = softmax and not is_last(T + 1)
                if lo_parts:
                    lo_part(U, q, 0)
                if softmax:
                    pool.wait_ge(g_hi_ready, U + 1)
                    nc.gpsimd.tensor_tensor(g_lo[q][:, :], g_scaled[:, :], g_hi[q][:, :].bitcast(f32),
                                            ALU.subtract).then_inc(g_ready, 1)
                if proj:
                    phi_part(T + 1, 1 - par)
                if lo_parts:
                    for k in range(1, CHUNKS):
                        lo_part(U, q, k)

            def theta(b):
                if b == 0:
                    phi_part(0, 0)

            schedule(period, theta, pool.Fori)

        @block.vector
        def _(dve):
            def take_projection(T, par, n, buf):
                dve.wait_ge(pair_filled, n + 1)
                if since(T, 2):
                    dve.wait_ge(g_hi_ready, T - 1)
                nc.vector.tensor_tensor(g_full[par][:, :], pair[buf][:, 1, 0:CI], bias_g[:, :], ALU.add)
                if since(T, 1):
                    dve.wait_ge(phi_ready, T)
                nc.vector.tensor_scalar(phi_full[:, :], pair[buf][:, 0, 0:P], bias_phi[:, :], None,
                                        ALU.add).then_inc(pair_drained, 1)

            def output_step(b, j):
                for h in range(2):
                    u = output_stage(b, 2 * j + h)
                    dve.wait_ge(stage_in[u % STAGES], 16 * (u // STAGES + 1))
                for o in range(HB):
                    n = output_use(b, j, o)
                    dve.wait_ge(pair_filled, n + 1)
                    for h in range(2):
                        columns = stage[output_stage(b, 2 * j + h) % STAGES][:, o, :]
                        last = nc.vector.scalar_tensor_tensor(out=columns, in0=pair[n % 2][:, h, 0:HALF],
                                                              scalar=bias_out[:, o:o + 1], in1=columns,
                                                              op0=ALU.add, op1=ALU.add)
                    last.then_inc(pair_drained, 1)

            def last_lo_part(k):
                q = LAST % 2
                dve.wait_ge(hi_ready, LAST * CHUNKS + k + 1)
                nc.vector.tensor_tensor(chunk(probs_lo, k), chunk(scores[q], k),
                                        chunk(probs_hi, k).bitcast(f32), ALU.subtract).then_inc(last_lo_ready, 1)

            def period(T, par, e):
                own, softmax, products, proj = runs(T)
                for j in range(STEPS):
                    if j == RECIP_AT and softmax:
                        dve.wait_ge(exp_done, T)
                        nc.vector.reciprocal(inv_sum[1 - par][:, :], row_sum[1 - par][:, :]).then_inc(inv_ready, 1)
                    if j == PROJ_AT and proj:
                        take_projection(T + 1, 1 - par, projection(T + 1, e), buffer(par, PROJ_AT))
                    if output_in(T) is not None:
                        output_step(output_in(T), j)
                    if own:
                        dve.wait_ge(pair_filled, use(T, j, e) + 1)
                        if since(T, 2) and j % 2 == 0:
                            dve.wait_ge(lo_ready, (T - 2) * CHUNKS + j // 2 + 1)
                        nc.vector.tensor_scalar(banks(scores[par], j), pair[step_buffer(T, par, j)][:, :, 0:HALF],
                                                0.0, None, ALU.add, ALU.max,
                                                accum_out=step_max[par][:, j:j + 1]).then_inc(pair_drained, 1)
                    if products:
                        dve.wait_ge(y_filled, (T - 2) * STEPS + j + 1)
                        if isinstance(T, int) and T % TILES == 2:
                            made = nc.vector.tensor_copy(banks(y_sum, j), y_pair[j % 2][:, :, 0:HALF])
                        else:
                            made = nc.vector.tensor_tensor(banks(y_sum, j), y_pair[j % 2][:, :, 0:HALF],
                                                           banks(y_sum, j), ALU.add)
                        made.then_inc(y_added, 1)
                    if is_last(T) and j:
                        output_step(B - 1, j - 1)
                if is_last(T):
                    output_step(B - 1, STEPS - 1)
                if is_last(T + 1):
                    for k in range(CHUNKS):
                        last_lo_part(k)
                if own:
                    dve.wait_ge(pair_drained, use(T, STEPS - 1, e) + 1)
                    nc.vector.tensor_reduce(neg_max[par][:, :], step_max[par][:, :], AX.X, ALU.max,
                                            negate=True).then_inc(max_ready, 1)

            def theta(b):
                if b == 0:
                    dve.wait_ge(theta_weights_in, 32)
                for j in range(STEPS):
                    n = theta_base(b) + j
                    dve.wait_ge(theta_hi_ready, b * STEPS + j + 1)
                    nc.vector.scalar_tensor_tensor(out=banks(theta_lo, j), in0=pair[n % 2][:, :, 0:HALF],
                                                   scalar=bias_theta[:, :], in1=banks(theta_hi, j).bitcast(f32),
                                                   op0=ALU.add, op1=ALU.subtract).then_inc(pair_drained, 1)
                if b == 0:
                    dve.wait_ge(weights_in, 16 * WEIGHTS)
                    take_projection(0, 0, STEPS, STEPS % 2)

            schedule(period, theta, dve.Fori)


_OUT = ((2, 256, 80, 80), 'float32')


def kernel(x, L0_conv_g_w, L0_conv_g_b, L0_conv_theta_w, L0_conv_theta_b, L0_conv_phi_w, L0_conv_phi_b,
           L0_conv_W_w, L0_conv_W_b):
    import numpy as _np
    import concourse.bacc as _bacc
    from concourse import mybir as _mybir
    from concourse.bass_utils import run_bass_kernel_spmd as _run

    nc = _bacc.Bacc("TRN2", target_bir_lowering=False, num_devices=1)
    given = {
        "x": x, "g_wT": L0_conv_g_w.T, "g_b": L0_conv_g_b, "theta_wT": L0_conv_theta_w.T,
        "theta_b": L0_conv_theta_b, "phi_wT": L0_conv_phi_w.T, "phi_b": L0_conv_phi_b,
        "out_wT": L0_conv_W_w.T, "out_b": L0_conv_W_b.reshape(-1, 128).T,
    }
    arrays, args = {}, []
    for name, value in given.items():
        a = _np.ascontiguousarray(value)
        arrays[f"in_{name}_dram"] = a
        args.append(nc.dram_tensor(f"in_{name}_dram", a.shape, _mybir.dt.from_np(a.dtype), kind="ExternalInput").ap())
    shape, dtype = _OUT
    args.append(nc.dram_tensor("out_0_dram", shape, _mybir.dt.from_np(_np.dtype(dtype)), kind="ExternalOutput").ap())
    build_non_local_block(nc, *args)
    r = _run(nc, [arrays], core_ids=[0])
    return r.results[0]["out_0_dram"]
```

```python
import concourse.bass as bass
from concourse import mybir
from contextlib import ExitStack


def build_non_local_block(nc, x, g_wT, g_b, theta_wT, theta_b, phi_wT, phi_b, out_wT, out_b, out):
    f32, f32r = mybir.dt.float32, mybir.dt.float32r
    ACT, ALU, AX = mybir.ActivationFunctionType, mybir.AluOpType, mybir.AxisListType

    B, C, H, W = x.shape
    N = H * W
    P = 128
    CI = theta_wT.shape[1]
    assert CI == P
    KC = C // P
    HB = C // P
    TILES = N // P
    BANK = 512
    PAIR = 2 * BANK
    STEPS = -(-N // PAIR)
    CHUNK_STEPS = ((0,), (1, 2), (3, 4), (5, 6))
    CHUNKS = len(CHUNK_STEPS)
    assert [j for steps in CHUNK_STEPS for j in steps] == list(range(STEPS))
    PROJ_AT = 4
    RECIP_AT = 3
    USES = STEPS + 1
    HALF = 400
    STRIP = 2 * HALF
    STRIPS = N // STRIP
    STAGES = 6
    BLOCKS = N // HALF

    xf = x.rearrange("b (k p) h w -> b p k (h w)", p=P)
    outf = out.rearrange("b (k p) h w -> b p k (h w)", p=P)

    ctx = ExitStack()
    with ctx:
        def sb(name, shape, dt=f32):
            return ctx.enter_context(nc.sbuf_tensor(name, shape, dt))

        def sem(name):
            return ctx.enter_context(nc.semaphore(name))

        w_theta = sb("w_theta", [P, KC, CI])
        w_phi = sb("w_phi", [P, KC, CI])
        w_g = sb("w_g", [P, KC, CI])
        w_out = sb("w_out", [CI, C])
        bias_theta = sb("bias_theta", [P, 1])
        bias_phi = sb("bias_phi", [P, 1])
        bias_out = sb("bias_out", [P, HB])
        bias_g = sb("bias_g", [P, CI])

        theta_hi = sb("theta_hi", [CI, N], f32r)
        theta_lo = sb("theta_lo", [CI, N], f32r)
        y_sum = sb("y_sum", [CI, N])
        scores = [sb(f"scores{i}", [P, N]) for i in range(2)]
        probs_hi = sb("probs_hi", [P, N], f32r)
        probs_lo = sb("probs_lo", [P, N], f32r)
        stage = sb("stage", [P, STAGES, KC, HALF])
        x_tile = [sb(f"x_tile{i}", [P, KC, P]) for i in range(2)]
        phi_full = sb("phi_full", [CI, P])
        phi_hi = [sb(f"phi_hi{i}", [CI, P], f32r) for i in range(2)]
        phi_lo = [sb(f"phi_lo{i}", [CI, P], f32r) for i in range(2)]
        g_full = [sb(f"g_full{i}", [P, CI]) for i in range(2)]
        g_scaled = sb("g_scaled", [P, CI])
        g_hi = [sb(f"g_hi{i}", [P, CI], f32r) for i in range(2)]
        g_lo = [sb(f"g_lo{i}", [P, CI], f32r) for i in range(2)]
        step_max = [sb(f"step_max{i}", [P, STEPS]) for i in range(2)]
        neg_max = [sb(f"neg_max{i}", [P, 1]) for i in range(2)]
        row_sum = [sb(f"row_sum{i}", [P, 1]) for i in range(2)]
        inv_sum = [sb(f"inv_sum{i}", [P, 1]) for i in range(2)]

        pair = [ctx.enter_context(nc.psum_tensor(f"pair{i}", [P, PAIR], f32)) for i in range(2)]
        y_pair = [ctx.enter_context(nc.psum_tensor(f"y_pair{i}", [P, PAIR], f32)) for i in range(2)]
        halves = [pair[i][:, :].rearrange("p (h c) -> p h c", h=2)[:, :, 0:HALF] for i in range(2)]

        theta_weights_in = sem("theta_weights_in")
        theta_bias_in = sem("theta_bias_in")
        weights_in = sem("weights_in")
        x_tile_in = [sem(f"x_tile_in{i}") for i in range(2)]
        stage_in = [sem(f"stage_in{i}") for i in range(STAGES)]
        stage_out = [sem(f"stage_out{i}") for i in range(STAGES)]
        spare_in = [sem(f"spare_in{i}") for i in range(N // (KC * STRIP))]
        spare_out = sem("spare_out")
        pair_filled = sem("pair_filled")
        pair_drained = sem("pair_drained")
        tile0_projected = sem("tile0_projected")
        tile0_taken = sem("tile0_taken")
        theta_hi_ready = sem("theta_hi_ready")
        phi_hi_ready = sem("phi_hi_ready")
        phi_ready = sem("phi_ready")
        max_ready = sem("max_ready")
        exp_done = sem("exp_done")
        inv_ready = sem("inv_ready")
        g_hi_ready = sem("g_hi_ready")
        g_ready = sem("g_ready")
        hi_ready = sem("hi_ready")
        lo_ready = sem("lo_ready")
        y_filled = sem("y_filled")
        y_added = sem("y_added")
        tail_lo_ready = sem("tail_lo_ready")

        LAST = B * TILES - 1
        assert HB * STRIPS % 2 == 0 and STRIPS % 2 == 0 and TILES % 2 == 0

        def start(j):
            return j * PAIR

        def end(j):
            return min(N, (j + 1) * PAIR)

        def step_of(column):
            return column // PAIR

        def chunk_of(j):
            return next((k for k, steps in enumerate(CHUNK_STEPS) if steps[0] == j), None)

        def strips_ahead(j):
            return sum(i * STRIP < end(j) for i in range(STRIPS))

        def strips_behind(j):
            return start(j) // STRIP

        def strips_after(j):
            return STRIPS if j == STEPS - 1 else strips_behind(j)

        FIRST_PROJ = 4
        WEIGHTS = 6

        def output_in(T):
            known = isinstance(T, int) and T > TILES and T <= LAST
            return T // TILES - 1 if known and T % TILES == 2 else None

        def runs(T):
            if not isinstance(T, int):
                return True, True, True, True
            return T <= LAST, 1 <= T <= LAST + 1, T >= 2, T < LAST

        def is_last(T):
            return isinstance(T, int) and T == LAST + 2

        VECTOR_STEPS = 2
        assert CHUNK_STEPS[0] == (0,) and CHUNK_STEPS[1] == (1, VECTOR_STEPS)

        def lo_chunks(U):
            last = isinstance(U, int) and U == LAST
            return [(k, max(steps[0], VECTOR_STEPS * last)) for k, steps in enumerate(CHUNK_STEPS) if k or not last]

        def lo_count(U, k):
            return U * CHUNKS + k + 1 - (isinstance(U, int) and U == LAST)

        def since(T, first):
            return not isinstance(T, int) or T >= first

        def extra(T):
            return sum(STRIPS * (T >= b * TILES) + HB * STRIPS * (T > b * TILES + 2) for b in range(1, B))

        def period_base(T, e):
            return STRIPS + USES * T + e

        def theta_base(b):
            return period_base(b * TILES, extra(b * TILES - 1)) if b else 0

        def theta_use(b, j):
            return theta_base(b) + j

        def outputs_ahead(T, j):
            return 0 if output_in(T) is None else HB * strips_ahead(j)

        def projection(T, e):
            return period_base(T - 1, e) + PROJ_AT + outputs_ahead(T - 1, PROJ_AT - 1)

        def use(T, j, e):
            late = j >= PROJ_AT and runs(T)[3]
            return period_base(T, e) + j + late + outputs_ahead(T, j)

        def output_use(b, j, o):
            T = (b + 1) * TILES + 2
            if b < B - 1:
                ahead = next(i for i in range(STEPS) if strips_ahead(i) > j)
                return use(T, ahead, extra(T)) - HB * (strips_ahead(ahead) - j) + o
            return period_base(LAST + 1, extra(LAST)) - 1 + HB * j + o

        def buffer(par, idx):
            return (STRIPS + par * USES + idx) % 2

        def step_buffer(T, par, j):
            return buffer(par, j + (j >= PROJ_AT and runs(T)[3]))

        def schedule(period, theta, Fori):
            for b in range(B):
                theta(b)
                first = b * TILES
                for T in range(first, first + 4):
                    period(T, T % 2, extra(T))
                with Fori(first + 4, first + TILES - 2 * (b == B - 1), 2) as T:
                    period(T, 0, extra(first + 4))
                    period(T + 1, 1, extra(first + 4))
            for T in range(LAST - 1, LAST + 3):
                period(T, T % 2, extra(LAST))

        def y_buffer(par, j):
            return (par * STEPS + j) % 2

        def columns_of(ap, j):
            return ap[:, start(j):end(j)]

        def chunk(ap, k):
            return ap[:, start(CHUNK_STEPS[k][0]):end(CHUNK_STEPS[k][-1])]

        def strip(ap, j):
            return ap[:, j * STRIP:(j + 1) * STRIP].rearrange("p (h c) -> p h c", h=2)

        def theta_stage(b, i):
            return BLOCKS * b + i

        def output_stage(b, i):
            return BLOCKS * (2 + b) + i - 2 * SPARES * (b == B - 1 and i >= STAGES + 2 * SPARES)

        SPARES = N // (KC * STRIP)
        spare = [scores[(LAST - 1) % 2][:, n * KC * STRIP:(n + 1) * KC * STRIP].rearrange("p (k c) -> p k c", k=KC)
                 for n in range(SPARES)]

        def spare_of(b, j):
            n = j - STAGES // 2
            return n if b == B - 1 and 0 <= n < SPARES else None

        assert B == 2 and BLOCKS % 2 == 0 and STAGES % 2 == 0

        block = ctx.enter_context(nc.Block())

        @block.sync
        def _(sp):
            def load_tile(b, t, par):
                T = b * TILES + t
                if since(T, 2):
                    sp.wait_ge(phi_ready, T - 1)
                sp.dma_start(x_tile[par][:, :, :], xf[b, :, :, bass.ds(t * P, P)]).then_inc(x_tile_in[par], 16)

            def load_stage(b, i, u):
                s = u % STAGES
                sp.dma_start(stage[:, s, :, :], xf[b, :, :, i * HALF:(i + 1) * HALF]).then_inc(stage_in[s], 16)

            def load_theta(b, i):
                u = theta_stage(b, i)
                if u >= STAGES:
                    n = u - STAGES
                    sp.wait_ge(pair_filled, theta_use(n // BLOCKS, n % BLOCKS // 2) + 1)
                load_stage(b, i, u)

            def stores_before(u):
                return 16 * sum(v % STAGES == u % STAGES for v in range(output_stage(0, 0), u))

            def load_residual(b, i):
                u = output_stage(b, i)
                if stores_before(u):
                    sp.wait_ge(stage_out[u % STAGES], stores_before(u))
                else:
                    sp.wait_ge(pair_filled, theta_use(B - 1, (BLOCKS + i - STAGES) // 2) + 1)
                load_stage(b, i, u)

            def load_spares():
                for n in range(SPARES):
                    j = n + STAGES // 2
                    last_step = step_of((n + 1) * KC * STRIP - 1)
                    k = next(k for k in range(CHUNKS) if last_step in CHUNK_STEPS[k])
                    sp.wait_ge(lo_ready, lo_count(LAST - 1, k))
                    sp.dma_start(spare[n][:, :, :], xf[B - 1, :, :, j * STRIP:(j + 1) * STRIP]
                                 ).then_inc(spare_in[n], 16)

            def output(b):
                for i in range(BLOCKS - 2 * (b == B - 1)):
                    if i % 2 == 0:
                        sp.wait_ge(pair_drained, output_use(b, i // 2, HB - 1) + 1)
                    n = spare_of(b, i // 2)
                    if n is None:
                        s = output_stage(b, i) % STAGES
                        sp.dma_start(outf[b, :, :, i * HALF:(i + 1) * HALF], stage[:, s, :, :]
                                     ).then_inc(stage_out[s], 16)
                    elif i % 2 == 0:
                        sp.dma_start(outf[b, :, :, i * HALF:i * HALF + STRIP], spare[n][:, :, :]
                                     ).then_inc(spare_out, 16)
                    if b < B - 1 and i >= 1 and i - 1 + STAGES < BLOCKS:
                        load_residual(b, i - 1 + STAGES)
                    if b == B - 1 and STAGES <= i < STAGES + 2:
                        load_residual(b, i + 2 * SPARES)

            load_theta(0, 0)
            load_theta(0, 1)
            load_tile(0, 0, 0)
            load_tile(0, 1, 1)
            for i in range(2, BLOCKS):
                load_theta(0, i)
            for i in range(STAGES):
                load_theta(1, i)
            load_tile(0, 2, 0)
            load_tile(0, 3, 1)
            with sp.Fori(4, TILES - 1, 2) as t:
                load_tile(0, t, 0)
                load_tile(0, t + 1, 1)
            for t in range(3):
                load_tile(1, t, t % 2)
            for i in range(STAGES, BLOCKS):
                load_theta(1, i)
            for i in range(STAGES):
                load_residual(0, i)
            for t in (3, 4):
                load_tile(1, t, t % 2)
            output(0)
            load_tile(1, 5, 1)
            with sp.Fori(6, TILES - 1, 2) as t:
                load_tile(1, t, 0)
                load_tile(1, t + 1, 1)
            for i in range(STAGES):
                load_residual(1, i)
            load_spares()
            output(1)
            s = output_stage(B - 1, BLOCKS - 2) % STAGES
            for o in range(HB):
                sp.wait_ge(pair_drained, output_use(B - 1, STRIPS - 1, o) + 1)
                sp.dma_start(outf[B - 1, :, o, N - STRIP:N].rearrange("p (h c) -> p h c", h=2),
                             stage[:, s:s + 2, o, :]).then_inc(stage_out[s + o], 16)
            sp.wait_ge(spare_out, 16 * SPARES)
            for s in range(STAGES):
                u = output_stage(B - 1, BLOCKS) + (s - output_stage(B - 1, BLOCKS)) % STAGES
                sp.wait_ge(stage_out[s], stores_before(u))

        @block.tensor
        def _(pe):
            def await_pair(n):
                if since(n, 2):
                    pe.wait_ge(pair_drained, n - 1)

            def product(into, parts, j):
                for i, (stationary, moving) in enumerate(parts):
                    for at in range(start(j), end(j), BANK):
                        width = min(BANK, N - at)
                        last = nc.tensor.matmul(into[:, at - start(j):at - start(j) + width], stationary[:, :],
                                                moving[:, at:at + width], start=i == 0, stop=i == len(parts) - 1)
                return last

            def project(T, par, into, signal):
                pe.wait_ge(x_tile_in[par], (T - par) * 8 + 16)
                for k in range(KC):
                    nc.tensor.matmul(into[:, 0:P], w_phi[:, k, :], x_tile[par][:, k, :],
                                     start=k == 0, stop=k == KC - 1)
                for k in range(KC):
                    last = nc.tensor.matmul(into[:, BANK:BANK + CI], x_tile[par][:, k, :], w_g[:, k, :],
                                            start=k == 0, stop=k == KC - 1)
                last.then_inc(signal, 1)

            def output_strip(b, j):
                pe.wait_ge(y_added, ((b + 1) * TILES - 1) * STEPS + step_of((j + 1) * STRIP - 1) + 1)
                for o in range(HB):
                    n = output_use(b, j, o)
                    await_pair(n)
                    for h in range(2):
                        at = j * STRIP + h * HALF
                        last = nc.tensor.matmul(halves[n % 2][:, h, :], w_out[:, o * P:(o + 1) * P],
                                                y_sum[:, at:at + HALF], start=True, stop=True)
                    last.then_inc(pair_filled, 1)

            def period(T, par, e):
                own, _, products, proj = runs(T)
                for j in range(STEPS):
                    if j == PROJ_AT and proj:
                        await_pair(projection(T + 1, e))
                        project(T + 1, 1 - par, pair[buffer(par, PROJ_AT)], pair_filled)
                    if output_in(T) is not None:
                        for i in range(strips_ahead(j - 1) if j else 0, strips_ahead(j)):
                            output_strip(output_in(T), i)
                    if own:
                        await_pair(use(T, j, e))
                        if j == 0:
                            pe.wait_ge(phi_ready, T + 1)
                        if isinstance(T, int) and T % TILES == 0:
                            pe.wait_ge(pair_drained, theta_use(T // TILES, (end(j) - 1) // STRIP) + 1)
                        parts = ((phi_lo[par], theta_hi), (phi_hi[par], theta_lo), (phi_hi[par], theta_hi))
                        product(pair[step_buffer(T, par, j)], parts, j).then_inc(pair_filled, 1)
                    if products:
                        if j == 0:
                            pe.wait_ge(g_ready, T - 1)
                        if is_last(T) and j < VECTOR_STEPS:
                            pe.wait_ge(tail_lo_ready, j + 1)
                        for k, first in lo_chunks(T - 2):
                            if j == first:
                                pe.wait_ge(lo_ready, lo_count(T - 2, k))
                        if since(T, 3) or j >= 2:
                            pe.wait_ge(y_added, (T - 2) * STEPS + j - 1)
                        parts = ((g_lo[par], probs_hi), (g_hi[par], probs_lo), (g_hi[par], probs_hi))
                        product(y_pair[y_buffer(par, j)], parts, j).then_inc(y_filled, 1)
                    if is_last(T):
                        for i in range(strips_after(j - 1) if j else 0, strips_after(j)):
                            output_strip(B - 1, i)

            def theta(b):
                if b == 0:
                    pe.wait_ge(theta_weights_in, 16)
                for j in range(STRIPS):
                    if b == 0 and j == FIRST_PROJ:
                        pe.wait_ge(weights_in, 16 * WEIGHTS)
                        project(0, 0, y_pair[0], tile0_projected)
                    n = theta_use(b, j)
                    await_pair(n)
                    for h in range(2):
                        u = theta_stage(b, 2 * j + h)
                        pe.wait_ge(stage_in[u % STAGES], 16 * (u // STAGES + 1))
                        for k in range(KC):
                            last = nc.tensor.matmul(halves[n % 2][:, h, :], w_theta[:, k, :],
                                                    stage[:, u % STAGES, k, :],
                                                    start=k == 0, stop=k == KC - 1)
                    last.then_inc(pair_filled, 1)

            schedule(period, theta, pe.Fori)

        @block.scalar
        def _(act):
            def load_weight(dst, src):
                return act.dma_start(dst[:, :, :], src.rearrange("(k p) c -> p k c", p=P))

            load_weight(w_theta, theta_wT).then_inc(theta_weights_in, 16)
            act.dma_start(bias_theta[:, :], theta_b.rearrange("(p a) -> p a", a=1)).then_inc(theta_bias_in, 16)
            load_weight(w_phi, phi_wT).then_inc(weights_in, 16)
            load_weight(w_g, g_wT).then_inc(weights_in, 16)
            act.dma_start(bias_phi[:, :], phi_b.rearrange("(p a) -> p a", a=1)).then_inc(weights_in, 16)
            act.dma_start(bias_g[:, :], g_b.partition_broadcast(P)).then_inc(weights_in, 16)
            act.dma_start(w_out[:, :], out_wT).then_inc(weights_in, 16)
            act.dma_start(bias_out[:, :], out_b).then_inc(weights_in, 16)

            def round_hi(U, q, k):
                act.wait_ge(exp_done, U + 1)
                if since(U, 1):
                    act.wait_ge(y_filled, (U - 1) * STEPS + CHUNK_STEPS[k][-1] + 1)
                nc.scalar.activation(chunk(probs_hi, k), chunk(scores[q], k), ACT.Copy).then_inc(hi_ready, 1)

            def round_phi(par):
                nc.scalar.activation(phi_hi[par][:, :], phi_full[:, :], ACT.Copy).then_inc(phi_hi_ready, 1)

            def scale_g(U, q):
                act.wait_ge(inv_ready, U + 1)
                if since(U, 1):
                    act.wait_ge(g_ready, U)
                nc.scalar.activation(g_scaled[:, :], g_full[q][:, :], ACT.Copy, scale=inv_sum[q][:, :])
                if since(U, 2):
                    act.wait_ge(y_filled, (U - 1) * STEPS)
                nc.scalar.activation(g_hi[q][:, :], g_full[q][:, :], ACT.Copy,
                                     scale=inv_sum[q][:, :]).then_inc(g_hi_ready, 1)

            def period(T, par, e):
                _, softmax, _, proj = runs(T)
                U, q = T - 1, 1 - par
                if softmax:
                    act.wait_ge(max_ready, U + 1)
                    nc.scalar.activation(scores[q][:, :], scores[q][:, :], ACT.Exp, bias=neg_max[q][:, :],
                                         accum_out=row_sum[q][:, :]).then_inc(exp_done, 1)
                    round_hi(U, q, 0)
                    scale_g(U, q)
                    round_hi(U, q, 1)
                if proj:
                    act.wait_ge(pair_drained, projection(T + 1, e) + 1)
                    round_phi(1 - par)
                if softmax:
                    round_hi(U, q, 2)
                    round_hi(U, q, 3)

            def theta(b):
                if b == 0:
                    act.wait_ge(theta_bias_in, 16)
                    nc.scalar.activation(row_sum[0][:, :], bias_theta[:, :], ACT.Exp)
                for j in range(STRIPS):
                    if b == 0 and j == FIRST_PROJ + 1:
                        act.wait_ge(tile0_taken, 1)
                        round_phi(0)
                    n = theta_use(b, j)
                    act.wait_ge(pair_filled, n + 1)
                    nc.scalar.activation(strip(theta_hi, j), halves[n % 2], ACT.Identity,
                                         bias=bias_theta[:, :]).then_inc(theta_hi_ready, 1)

            schedule(period, theta, act.Fori)

        @block.gpsimd
        def _(pool):
            def lo_part(U, q, k, first):
                columns = slice(start(first), end(CHUNK_STEPS[k][-1]))
                pool.wait_ge(hi_ready, U * CHUNKS + k + 1)
                nc.gpsimd.tensor_tensor(probs_lo[:, columns], scores[q][:, columns],
                                        probs_hi[:, columns].bitcast(f32), ALU.subtract).then_inc(lo_ready, 1)

            def phi_part(T, par):
                pool.wait_ge(phi_hi_ready, T + 1)
                nc.gpsimd.tensor_tensor(phi_lo[par][:, :], phi_full[:, :], phi_hi[par][:, :].bitcast(f32),
                                        ALU.subtract).then_inc(phi_ready, 1)

            def period(T, par, e):
                _, softmax, _, proj = runs(T)
                U, q = T - 1, 1 - par
                parts = lo_chunks(U)
                if softmax:
                    if parts[0][0] == 0:
                        lo_part(U, q, *parts.pop(0))
                    pool.wait_ge(g_hi_ready, U + 1)
                    nc.gpsimd.tensor_tensor(g_lo[q][:, :], g_scaled[:, :], g_hi[q][:, :].bitcast(f32),
                                            ALU.subtract).then_inc(g_ready, 1)
                if proj:
                    phi_part(T + 1, 1 - par)
                if softmax:
                    for k, first in parts:
                        lo_part(U, q, k, first)

            def theta(b):
                if b == 0:
                    phi_part(0, 0)

            schedule(period, theta, pool.Fori)

        @block.vector
        def _(dve):
            def take_projection(T, par, made, signal):
                if since(T, 2):
                    dve.wait_ge(g_hi_ready, T - 1)
                nc.vector.tensor_tensor(g_full[par][:, :], made[:, BANK:BANK + CI], bias_g[:, :], ALU.add)
                if since(T, 1):
                    dve.wait_ge(phi_ready, T)
                nc.vector.tensor_scalar(phi_full[:, :], made[:, 0:P], bias_phi[:, :], None,
                                        ALU.add).then_inc(signal, 1)

            def output_strip(b, j):
                n = spare_of(b, j)
                if n is None:
                    for h in range(2):
                        u = output_stage(b, 2 * j + h)
                        dve.wait_ge(stage_in[u % STAGES], 16 * (u // STAGES + 1))
                    s = output_stage(b, 2 * j) % STAGES
                    parts = [stage[:, s:s + 2, o, :] for o in range(HB)]
                else:
                    dve.wait_ge(spare_in[n], 16)
                    parts = [spare[n][:, o, :].rearrange("p (h c) -> p h c", h=2) for o in range(HB)]
                for o, columns in enumerate(parts):
                    n = output_use(b, j, o)
                    dve.wait_ge(pair_filled, n + 1)
                    nc.vector.scalar_tensor_tensor(out=columns, in0=halves[n % 2],
                                                   scalar=bias_out[:, o:o + 1], in1=columns,
                                                   op0=ALU.add, op1=ALU.add).then_inc(pair_drained, 1)

            def tail_lo_part(j):
                k = next(k for k in range(CHUNKS) if j in CHUNK_STEPS[k])
                dve.wait_ge(hi_ready, LAST * CHUNKS + k + 1)
                nc.vector.tensor_tensor(columns_of(probs_lo, j), columns_of(scores[LAST % 2], j),
                                        columns_of(probs_hi, j).bitcast(f32), ALU.subtract).then_inc(tail_lo_ready, 1)

            def invert_sum(T, q):
                dve.wait_ge(exp_done, T)
                nc.vector.reciprocal(inv_sum[q][:, :], row_sum[q][:, :]).then_inc(inv_ready, 1)

            def period(T, par, e):
                own, softmax, products, proj = runs(T)
                for j in range(STEPS):
                    if is_last(T + 1) and j == STEPS - 3:
                        invert_sum(T, 1 - par)
                    if is_last(T + 1) and j == STEPS - 2:
                        tail_lo_part(0)
                    if j == RECIP_AT and own and softmax:
                        invert_sum(T, 1 - par)
                    if j == PROJ_AT and proj:
                        dve.wait_ge(pair_filled, projection(T + 1, e) + 1)
                        take_projection(T + 1, 1 - par, pair[buffer(par, PROJ_AT)], pair_drained)
                    if output_in(T) is not None:
                        for i in range(strips_ahead(j - 1) if j else 0, strips_ahead(j)):
                            output_strip(output_in(T), i)
                    if own:
                        dve.wait_ge(pair_filled, use(T, j, e) + 1)
                        if since(T, 2) and chunk_of(j) is not None:
                            dve.wait_ge(lo_ready, (T - 2) * CHUNKS + chunk_of(j) + 1)
                        nc.vector.tensor_scalar(columns_of(scores[par], j),
                                                pair[step_buffer(T, par, j)][:, 0:end(j) - start(j)],
                                                0.0, None, ALU.add, ALU.max,
                                                accum_out=step_max[par][:, j:j + 1]).then_inc(pair_drained, 1)
                    if products:
                        dve.wait_ge(y_filled, (T - 2) * STEPS + j + 1)
                        products_of = y_pair[y_buffer(par, j)][:, 0:end(j) - start(j)]
                        if isinstance(T, int) and T % TILES == 2:
                            made = nc.vector.tensor_copy(columns_of(y_sum, j), products_of)
                        else:
                            made = nc.vector.tensor_tensor(columns_of(y_sum, j), products_of,
                                                           columns_of(y_sum, j), ALU.add)
                        made.then_inc(y_added, 1)
                    if is_last(T):
                        for i in range(strips_after(j - 1) if j else 0, strips_after(j)):
                            output_strip(B - 1, i)
                if is_last(T + 1):
                    tail_lo_part(1)
                if own:
                    dve.wait_ge(pair_drained, use(T, STEPS - 1, e) + 1)
                    nc.vector.tensor_reduce(neg_max[par][:, :], step_max[par][:, :], AX.X, ALU.max,
                                            negate=True).then_inc(max_ready, 1)

            def theta(b):
                if b == 0:
                    dve.wait_ge(theta_bias_in, 16)
                for j in range(STRIPS):
                    if b == 0 and j == FIRST_PROJ:
                        dve.wait_ge(weights_in, 16 * WEIGHTS)
                        dve.wait_ge(tile0_projected, 1)
                        take_projection(0, 0, y_pair[0], tile0_taken)
                    n = theta_use(b, j)
                    dve.wait_ge(theta_hi_ready, b * STRIPS + j + 1)
                    nc.vector.scalar_tensor_tensor(out=strip(theta_lo, j), in0=halves[n % 2],
                                                   scalar=bias_theta[:, :], in1=strip(theta_hi, j).bitcast(f32),
                                                   op0=ALU.add, op1=ALU.subtract).then_inc(pair_drained, 1)

            schedule(period, theta, dve.Fori)


_OUT = ((2, 256, 80, 80), 'float32')


def kernel(x, L0_conv_g_w, L0_conv_g_b, L0_conv_theta_w, L0_conv_theta_b, L0_conv_phi_w, L0_conv_phi_b,
           L0_conv_W_w, L0_conv_W_b):
    import numpy as _np
    import concourse.bacc as _bacc
    from concourse import mybir as _mybir
    from concourse.bass_utils import run_bass_kernel_spmd as _run

    nc = _bacc.Bacc("TRN2", target_bir_lowering=False, num_devices=1)
    given = {
        "x": x, "g_wT": L0_conv_g_w.T, "g_b": L0_conv_g_b, "theta_wT": L0_conv_theta_w.T,
        "theta_b": L0_conv_theta_b, "phi_wT": L0_conv_phi_w.T, "phi_b": L0_conv_phi_b,
        "out_wT": L0_conv_W_w.T, "out_b": L0_conv_W_b.reshape(-1, 128).T,
    }
    arrays, args = {}, []
    for name, value in given.items():
        a = _np.ascontiguousarray(value)
        arrays[f"in_{name}_dram"] = a
        args.append(nc.dram_tensor(f"in_{name}_dram", a.shape, _mybir.dt.from_np(a.dtype), kind="ExternalInput").ap())
    shape, dtype = _OUT
    args.append(nc.dram_tensor("out_0_dram", shape, _mybir.dt.from_np(_np.dtype(dtype)), kind="ExternalOutput").ap())
    build_non_local_block(nc, *args)
    r = _run(nc, [arrays], core_ids=[0])
    return r.results[0]["out_0_dram"]
```
